# Optimizing a Trainium2 kernel written in Bass

```python
import numpy as np
import jax
import jax.numpy as jnp

def _softmax(x, axis=-1):
    return jax.nn.softmax(x, axis=axis)

def _gelu(x):
    return jax.nn.gelu(x, approximate=True)

def _silu(x):
    return jax.nn.silu(x)

def _sigmoid(x):
    return jax.nn.sigmoid(x)

def _layernorm(x, axis=-1, eps=1e-05):
    m = jnp.mean(x, axis=axis, keepdims=True)
    v = jnp.var(x, axis=axis, keepdims=True)
    return (x - m) / jnp.sqrt(v + eps)

def _scatter_add(tgt, idx, src, axis=0):
    return tgt.at[idx].add(src)

def _segment_sum(src, seg, n):
    return jax.ops.segment_sum(src, seg, n)
kernel_name = 'mk_dlrm_tower_d1_rec_r8_f8fbd5'

def setup_inputs(seed: int=0):
    np.random.seed(seed)
    _w = jnp.asarray

    def _rec_inputs():
        import jax
        import jax.numpy as jnp
        _tk = jax.random.key(seed)
        ids = jnp.stack([jax.random.randint(jax.random.fold_in(_tk, 200 + f), (512,), 0, v, jnp.int32) for f, v in enumerate([1000, 1250, 12500, 125000, 1250, 1000, 1250, 1250, 1000, 12500, 1250, 12500, 1000, 12500, 12500, 1000, 12500, 12500, 12500, 1000, 1250, 1000, 1250, 1250, 1000, 1250])], axis=1)
        tbl_0 = 0.05 * jax.random.normal(jax.random.fold_in(_tk, 500 + 0), (1000, 128), jnp.float32)
        tbl_1 = 0.05 * jax.random.normal(jax.random.fold_in(_tk, 500 + 1), (1250, 128), jnp.float32)
        tbl_2 = 0.05 * jax.random.normal(jax.random.fold_in(_tk, 500 + 2), (12500, 128), jnp.float32)
        tbl_3 = 0.05 * jax.random.normal(jax.random.fold_in(_tk, 500 + 3), (125000, 128), jnp.float32)
        tbl_4 = 0.05 * jax.random.normal(jax.random.fold_in(_tk, 500 + 4), (1250, 128), jnp.float32)
        tbl_5 = 0.05 * jax.random.normal(jax.random.fold_in(_tk, 500 + 5), (1000, 128), jnp.float32)
        tbl_6 = 0.05 * jax.random.normal(jax.random.fold_in(_tk, 500 + 6), (1250, 128), jnp.float32)
        tbl_7 = 0.05 * jax.random.normal(jax.random.fold_in(_tk, 500 + 7), (1250, 128), jnp.float32)
        tbl_8 = 0.05 * jax.random.normal(jax.random.fold_in(_tk, 500 + 8), (1000, 128), jnp.float32)
        tbl_9 = 0.05 * jax.random.normal(jax.random.fold_in(_tk, 500 + 9), (12500, 128), jnp.float32)
        tbl_10 = 0.05 * jax.random.normal(jax.random.fold_in(_tk, 500 + 10), (1250, 128), jnp.float32)
        tbl_11 = 0.05 * jax.random.normal(jax.random.fold_in(_tk, 500 + 11), (12500, 128), jnp.float32)
        tbl_12 = 0.05 * jax.random.normal(jax.random.fold_in(_tk, 500 + 12), (1000, 128), jnp.float32)
        tbl_13 = 0.05 * jax.random.normal(jax.random.fold_in(_tk, 500 + 13), (12500, 128), jnp.float32)
        tbl_14 = 0.05 * jax.random.normal(jax.random.fold_in(_tk, 500 + 14), (12500, 128), jnp.float32)
        tbl_15 = 0.05 * jax.random.normal(jax.random.fold_in(_tk, 500 + 15), (1000, 128), jnp.float32)
        tbl_16 = 0.05 * jax.random.normal(jax.random.fold_in(_tk, 500 + 16), (12500, 128), jnp.float32)
        tbl_17 = 0.05 * jax.random.normal(jax.random.fold_in(_tk, 500 + 17), (12500, 128), jnp.float32)
        tbl_18 = 0.05 * jax.random.normal(jax.random.fold_in(_tk, 500 + 18), (12500, 128), jnp.float32)
        tbl_19 = 0.05 * jax.random.normal(jax.random.fold_in(_tk, 500 + 19), (1000, 128), jnp.float32)
        tbl_20 = 0.05 * jax.random.normal(jax.random.fold_in(_tk, 500 + 20), (1250, 128), jnp.float32)
        tbl_21 = 0.05 * jax.random.normal(jax.random.fold_in(_tk, 500 + 21), (1000, 128), jnp.float32)
        tbl_22 = 0.05 * jax.random.normal(jax.random.fold_in(_tk, 500 + 22), (1250, 128), jnp.float32)
        tbl_23 = 0.05 * jax.random.normal(jax.random.fold_in(_tk, 500 + 23), (1250, 128), jnp.float32)
        tbl_24 = 0.05 * jax.random.normal(jax.random.fold_in(_tk, 500 + 24), (1000, 128), jnp.float32)
        tbl_25 = 0.05 * jax.random.normal(jax.random.fold_in(_tk, 500 + 25), (1250, 128), jnp.float32)
        _rk = jax.random.fold_in(_tk, 7)
        r_dense_x = -0.000514642 + 1.00011 * jax.random.normal(jax.random.fold_in(_rk, 101), (512, 128), jnp.float32)
        W_top1 = 0.0456912 * jax.random.normal(jax.random.fold_in(_tk, 801), (479, 512), jnp.float32)
        W_top2 = 0.0441942 * jax.random.normal(jax.random.fold_in(_tk, 802), (512, 256), jnp.float32)
        W_top3 = 0.0625 * jax.random.normal(jax.random.fold_in(_tk, 803), (256, 1), jnp.float32)
        b_top1 = jnp.zeros((512,), jnp.float32)
        b_top2 = jnp.zeros((256,), jnp.float32)
        return (r_dense_x, ids, tbl_0, tbl_1, tbl_2, tbl_3, tbl_4, tbl_5, tbl_6, tbl_7, tbl_8, tbl_9, tbl_10, tbl_11, tbl_12, tbl_13, tbl_14, tbl_15, tbl_16, tbl_17, tbl_18, tbl_19, tbl_20, tbl_21, tbl_22, tbl_23, tbl_24, tbl_25, W_top1, b_top1, W_top2, b_top2, W_top3)
    r_dense_x, ids, tbl_0, tbl_1, tbl_2, tbl_3, tbl_4, tbl_5, tbl_6, tbl_7, tbl_8, tbl_9, tbl_10, tbl_11, tbl_12, tbl_13, tbl_14, tbl_15, tbl_16, tbl_17, tbl_18, tbl_19, tbl_20, tbl_21, tbl_22, tbl_23, tbl_24, tbl_25, W_top1, b_top1, W_top2, b_top2, W_top3 = _rec_inputs()

    def _L0_rec_setup():
        import jax, jax.numpy as jnp
        import numpy as np
        F = 26
        D = 128
        B = 2048
        _TRIU_I, _TRIU_J = np.triu_indices(F + 1, k=1)
        _TRIU_I = jnp.asarray(_TRIU_I)
        _TRIU_J = jnp.asarray(_TRIU_J)
        key = jax.random.key(seed)
        k1, k2 = jax.random.split(key)
        sparse_x = jax.random.normal(k1, (B, F, D), dtype=jnp.float32)
        dense_x = jax.random.normal(k2, (B, D), dtype=jnp.float32)
        return {'sparse_x': sparse_x, 'dense_x': dense_x}
    _L0_rec_all = _L0_rec_setup()
    _L0_rec_in = {k: v for k, v in _L0_rec_all.items() if k in ()}
    del _L0_rec_all
    return {'r_dense_x': r_dense_x, 'ids': ids, 'tbl_0': tbl_0, 'tbl_1': tbl_1, 'tbl_2': tbl_2, 'tbl_3': tbl_3, 'tbl_4': tbl_4, 'tbl_5': tbl_5, 'tbl_6': tbl_6, 'tbl_7': tbl_7, 'tbl_8': tbl_8, 'tbl_9': tbl_9, 'tbl_10': tbl_10, 'tbl_11': tbl_11, 'tbl_12': tbl_12, 'tbl_13': tbl_13, 'tbl_14': tbl_14, 'tbl_15': tbl_15, 'tbl_16': tbl_16, 'tbl_17': tbl_17, 'tbl_18': tbl_18, 'tbl_19': tbl_19, 'tbl_20': tbl_20, 'tbl_21': tbl_21, 'tbl_22': tbl_22, 'tbl_23': tbl_23, 'tbl_24': tbl_24, 'tbl_25': tbl_25, 'W_top1': W_top1, 'b_top1': b_top1, 'W_top2': W_top2, 'b_top2': b_top2, 'W_top3': W_top3}

def reference(r_dense_x, ids, tbl_0, tbl_1, tbl_2, tbl_3, tbl_4, tbl_5, tbl_6, tbl_7, tbl_8, tbl_9, tbl_10, tbl_11, tbl_12, tbl_13, tbl_14, tbl_15, tbl_16, tbl_17, tbl_18, tbl_19, tbl_20, tbl_21, tbl_22, tbl_23, tbl_24, tbl_25, W_top1, b_top1, W_top2, b_top2, W_top3):
    import jax
    import jax.numpy as jnp

    def _L0_rec_ref(sparse_x, dense_x):
        import jax, jax.numpy as jnp
        import numpy as np
        F = 26
        D = 128
        B = 2048
        _TRIU_I, _TRIU_J = np.triu_indices(F + 1, k=1)
        _TRIU_I = jnp.asarray(_TRIU_I)
        _TRIU_J = jnp.asarray(_TRIU_J)
        combined = jnp.concatenate([sparse_x, dense_x[:, None, :]], axis=1)
        interact = jnp.einsum('bfd,bgd->bfg', combined, combined)
        return interact[:, _TRIU_I, _TRIU_J]
    e = jnp.stack([tbl_0[ids[:, 0]], tbl_1[ids[:, 1]], tbl_2[ids[:, 2]], tbl_3[ids[:, 3]], tbl_4[ids[:, 4]], tbl_5[ids[:, 5]], tbl_6[ids[:, 6]], tbl_7[ids[:, 7]], tbl_8[ids[:, 8]], tbl_9[ids[:, 9]], tbl_10[ids[:, 10]], tbl_11[ids[:, 11]], tbl_12[ids[:, 12]], tbl_13[ids[:, 13]], tbl_14[ids[:, 14]], tbl_15[ids[:, 15]], tbl_16[ids[:, 16]], tbl_17[ids[:, 17]], tbl_18[ids[:, 18]], tbl_19[ids[:, 19]], tbl_20[ids[:, 20]], tbl_21[ids[:, 21]], tbl_22[ids[:, 22]], tbl_23[ids[:, 23]], tbl_24[ids[:, 24]], tbl_25[ids[:, 25]]], axis=1)
    z = _L0_rec_ref(e, r_dense_x)
    z = z.reshape(z.shape[0], -1)
    h = jnp.concatenate([z, r_dense_x], axis=1)
    h = jnp.maximum(h @ W_top1 + b_top1, 0.0)
    h = jnp.maximum(h @ W_top2 + b_top2, 0.0)
    y = h @ W_top3
    return y

_drawn_inputs = setup_inputs


def setup_inputs(seed=0):
    import zlib

    import numpy as np

    out = dict(_drawn_inputs(seed))
    spreads = {'b_top1': (0.0, 0.1), 'b_top2': (0.0, 0.1)}
    factors = {}
    for name, (base, spread) in spreads.items():
        noise = np.random.default_rng([zlib.crc32(name.encode()), seed]).standard_normal(out[name].shape)
        drawn = base * np.exp(spread * noise) if base else spread * noise
        out[name] = jnp.asarray(drawn.astype(out[name].dtype))
    for name, factor in factors.items():
        out[name] = (out[name] * factor).astype(out[name].dtype)
    return out
```

```python
from contextlib import ExitStack

import concourse.bass as bass
from concourse import mybir

F32 = mybir.dt.float32
I32 = mybir.dt.int32
ALU = mybir.AluOpType
ACT = mybir.ActivationFunctionType

P = 128
B, D = 512, 128
FIELDS = 26
VECS = FIELDS + 1
QUAD = 32
TILES = B // P
GROUP = P // QUAD
GROUPS = P // GROUP
STEPS = (VECS + GROUP - 1) // GROUP
COLS = STEPS * GROUP
FILL = 8
FILLS = GROUPS // FILL
N1, N2 = 512, 256
C1, C2 = N1 // P, N2 // P
BLOCKS = [list(range(k, min(k + 4, VECS))) for k in range(0, VECS, 4)]
HALF = 15
HALF_BLOCK = 4


def build(nc, x, ids, tables, w1_pairs, w1_dense, b1, w2, b2, w3, out):
    x_v = x.rearrange("(p t) d -> p t d", t=TILES)
    ids_v = ids.rearrange("(p t) f -> p t f", t=TILES)
    with ExitStack() as ctx:
        def sb(name, shape, dt=F32):
            return ctx.enter_context(nc.sbuf_tensor(name, shape, dt))

        def pb(name, shape):
            return ctx.enter_context(nc.psum_tensor(name, shape, F32))

        def sem(name):
            return ctx.enter_context(nc.semaphore(name))

        ident = sb("ident", [P, P])
        idx = sb("idx", [P, FIELDS], I32)
        rows = sb("rows", [P, VECS, D])
        xt = sb("xt", [D, P, QUAD])
        zt = sb("zt", [P, STEPS, P])
        w1p_sb = sb("w1p_sb", [P, STEPS, N1])
        w1d_sb = sb("w1d_sb", [P, N1])
        w2_sb = sb("w2_sb", [P, C1, N2])
        w3_sb = sb("w3_sb", [P, C2])
        b1_sb = sb("b1_sb", [P, C1])
        b2_sb = sb("b2_sb", [P, C2])
        h1 = sb("h1", [P, C1, P])
        h2 = sb("h2", [P, C2, P])
        y_sb = sb("y_sb", [P, TILES])

        tp = pb("tp", [P, 2, 4, P])
        gram = pb("gram", [P, 2, FILL, P])
        ps1 = pb("ps1", [P, C1, P])
        ps2 = pb("ps2", [P, 4, P])

        s_sp = sem("sp_cleared")
        s_pool = sem("pool_cleared")
        s_zero = sem("ident_zeroed")
        s_ident = sem("ident_ready")
        s_pad = sem("pads_zeroed")
        s_idx = [sem("idx_low_in"), sem("idx_high_in")]
        s_dense = sem("dense_in")
        s_rows = [sem(f"rows_in_{k}") for k in range(len(BLOCKS))]
        s_w1 = sem("w1_in")
        s_w2 = sem("w2_in")
        s_tr = [sem(f"transposed_{k}") for k in range(len(BLOCKS))]
        s_xt = sem("xt_ready")
        s_gram = sem("gram_ready")
        s_za = sem("z_copied_act")
        s_zv = sem("z_copied_dve")
        s_l1 = sem("layer1_ready")
        s_h1 = sem("h1_ready")
        s_l2 = sem("layer2_ready")
        s_h2 = sem("h2_ready")
        s_l3 = sem("layer3_ready")
        s_y = sem("y_ready")
        s_out = sem("out_written")
        block = ctx.enter_context(nc.Block())

        nb = len(BLOCKS)
        gathers = [16 * sum(p > 0 for p in blk) for blk in BLOCKS]

        def z_copies(eng, k, samples, done):
            for s in samples:
                for q in range(GROUP):
                    src = gram[QUAD * s:QUAD * s + QUAD, k % 2, :, s * COLS + q:(s + 1) * COLS:GROUP]
                    dst = zt[QUAD * q:QUAD * q + QUAD, :, GROUP * FILL * k + s:GROUP * FILL * (k + 1):GROUP]
                    dst = dst.rearrange("p j g -> p g j")
                    last = (eng.activation(dst, src, ACT.Copy) if done is s_za else eng.tensor_copy(dst, src))
            last.then_inc(done, 1)

        @block.sync
        def _(sp):
            with sp.Fori(0, TILES) as t:
                for k in range(HALF_BLOCK):
                    sp.wait_ge(s_tr[k], t + 1)
                sp.sem_inc(s_sp, 1)
                sp.dma_start(idx[:, 0:HALF], ids_v[:, bass.ds(t, 1), 0:HALF]).then_inc(s_idx[0], 16)
                sp.dma_start(rows[:, 0, :], x_v[:, bass.ds(t, 1), :]).then_inc(s_dense, 16)
                for k in range(HALF_BLOCK, nb):
                    sp.wait_ge(s_tr[k], t + 1)
                sp.sem_inc(s_sp, 1)
                sp.dma_start(idx[:, HALF:FIELDS], ids_v[:, bass.ds(t, 1), HALF:FIELDS]).then_inc(s_idx[1], 16)
            sp.wait_ge(s_y, TILES + 1)
            sp.dma_start(out.rearrange("(p t) o -> p (t o)", t=TILES), y_sb[:, :]).then_inc(s_out, 16)
            sp.wait_ge(s_out, 16)

        @block.gpsimd
        def _(pool):
            pool.memset(ident[:, :], 0.0).then_inc(s_zero, 1)
            pool.wait_ge(s_zero, 1)
            pool.affine_select(out=ident[:, :], in_=ident[:, :], compare_op=ALU.not_equal, fill=1.0,
                               base=0, pattern=[[-1, P]], channel_multiplier=1).then_inc(s_ident, 1)
            with pool.Fori(0, TILES) as t:
                for k, blk in enumerate(BLOCKS):
                    if k in (0, HALF_BLOCK):
                        pool.wait_ge(s_idx[k // HALF_BLOCK], 16 * t + 16)
                        for m in (range(HALF_BLOCK) if k == 0 else range(HALF_BLOCK, nb)):
                            pool.wait_ge(s_tr[m], t + 1)
                        pool.sem_inc(s_pool, 1)
                    for p in blk:
                        if p > 0:
                            f = p - 1
                            pool.indirect_dma_start(
                                rows[:, p, :], None, tables[f][:, :],
                                bass.IndirectOffsetOnAxis(ap=idx[:, f:f + 1], axis=0),
                            ).then_inc(s_rows[k], 16)

        @block.scalar
        def _(act):
            act.wait_ge(s_idx[0], 16)
            act.sem_inc(s_za, 1)
            act.sem_inc(s_h1, 1)
            act.sem_inc(s_y, 1)
            act.dma_start(w1p_sb[:, :, :], w1_pairs).then_inc(s_w1, 16)
            act.dma_start(w1d_sb[:, :], w1_dense).then_inc(s_w1, 16)
            act.dma_start(w2_sb[:, :, :], w2.rearrange("(c p) n -> p c n", p=P)).then_inc(s_w2, 16)
            act.dma_start(w3_sb[:, :], w3).then_inc(s_w2, 16)
            act.dma_start(b1_sb[:, :], b1).then_inc(s_w2, 16)
            act.dma_start(b2_sb[:, :], b2).then_inc(s_w2, 16)
            act.wait_ge(s_w2, 64)
            with act.Fori(0, TILES) as t:
                act.wait_ge(s_l1, t + 1)
                for k in range(FILLS):
                    act.wait_ge(s_gram, FILLS * t + (k + 2))
                    z_copies(act, k, (0, 1), s_za)
                act.wait_ge(s_l1, t + 2)
                for c in range(C1):
                    act.activation(h1[:, c, :], ps1[:, c, :], ACT.Relu, bias=b1_sb[:, c:c + 1]).then_inc(s_h1, 1)
                act.wait_ge(s_l2, t + 1)
                for c in range(C2):
                    act.activation(h2[:, c, :], ps2[:, c, :], ACT.Relu, bias=b2_sb[:, c:c + 1]).then_inc(s_h2, 1)
                act.wait_ge(s_l3, t + 1)
                act.activation(y_sb[:, bass.ds(t, 1)], ps2[:, C2, 0:1], ACT.Copy).then_inc(s_y, 1)

        @block.vector
        def _(dve):
            dve.sem_inc(s_xt, 1)
            dve.sem_inc(s_zv, 1)
            dve.memset(xt[:, :, VECS:QUAD], 0.0).then_inc(s_pad, 1)
            with dve.Fori(0, TILES) as t:
                dve.wait_ge(s_gram, FILLS * t + 1)
                for k, blk in enumerate(BLOCKS):
                    dve.wait_ge(s_tr[k], t + 2)
                    dve.tensor_copy(xt[:, :, blk[0]:blk[-1] + 1],
                                    tp[:, k % 2, 0:len(blk), :].rearrange("d f b -> d b f")).then_inc(s_xt, 1)
                dve.wait_ge(s_l1, t + 1)
                for k in range(FILLS):
                    dve.wait_ge(s_gram, FILLS * t + (k + 2))
                    z_copies(dve, k, (2, 3), s_zv)

        @block.tensor
        def _(pe):
            for k in range(nb):
                pe.sem_inc(s_tr[k], 1)
            pe.sem_inc(s_gram, 1)
            pe.sem_inc(s_l1, 1)
            pe.wait_ge(s_ident, 1)
            with pe.Fori(0, TILES) as t:
                for k, blk in enumerate(BLOCKS):
                    if k == 0:
                        pe.wait_ge(s_dense, 16 * t + 16)
                    pe.wait_ge(s_rows[k], gathers[k] * t + gathers[k])
                    if k < 2:
                        pe.wait_ge(s_xt, nb * t + 1)
                    else:
                        pe.wait_ge(s_xt, nb * t + k)
                    for i, p in enumerate(blk):
                        last = pe.transpose(tp[:, k % 2, i, :], rows[:, p, :], ident[:, :])
                    last.then_inc(s_tr[k], 1)
                pe.wait_ge(s_xt, nb * t + (nb + 1))
                pe.wait_ge(s_pad, 1)
                for k in range(FILLS):
                    prev = FILLS * t + (1 if k < 2 else k)
                    pe.wait_ge(s_za, prev)
                    pe.wait_ge(s_zv, prev)
                    for g in range(FILL):
                        b0 = (k * FILL + g) * GROUP
                        last = pe.matmul(
                            gram[:, k % 2, g, 0:GROUP * COLS].rearrange("p (s v) -> p s v", s=GROUP),
                            xt[:, b0:b0 + GROUP, :].rearrange("d s v -> d (s v)"),
                            xt[:, b0:b0 + GROUP, 0:COLS], start=True, stop=True)
                    last.then_inc(s_gram, 1)
                pe.wait_ge(s_w1, 32)
                pe.wait_ge(s_h1, C1 * t + 1)
                pe.wait_ge(s_za, FILLS * t + (FILLS + 1))
                pe.wait_ge(s_zv, FILLS * t + (FILLS + 1))
                for c in range(C1):
                    pe.matmul(ps1[:, c, :], w1d_sb[:, c * P:(c + 1) * P], xt[:, :, 0], start=True, stop=False)
                    for j in range(STEPS):
                        last = pe.matmul(ps1[:, c, :], w1p_sb[:, j, c * P:(c + 1) * P], zt[:, j, :],
                                         start=False, stop=j == STEPS - 1)
                last.then_inc(s_l1, 1)
                pe.wait_ge(s_w2, 64)
                pe.wait_ge(s_h1, C1 * t + (C1 + 1))
                pe.wait_ge(s_y, t + 1)
                for c in range(C2):
                    for j in range(C1):
                        last = pe.matmul(ps2[:, c, :], w2_sb[:, j, c * P:(c + 1) * P], h1[:, j, :],
                                         start=j == 0, stop=j == C1 - 1)
                last.then_inc(s_l2, 1)
                pe.wait_ge(s_h2, C2 * t + C2)
                for c in range(C2):
                    last = pe.matmul(ps2[:, C2, 0:1], h2[:, c, :], w3_sb[:, c:c + 1], start=c == 0, stop=c == C2 - 1)
                last.then_inc(s_l3, 1)


def pair_rows():
    feature = [FIELDS] + list(range(FIELDS))
    row = {}
    for i in range(VECS):
        for j in range(i + 1, VECS):
            row[i, j] = len(row)
    nothing = VECS * (VECS - 1) // 2 + D
    out = [[nothing] * STEPS for _ in range(P)]
    for q in range(GROUP):
        for a in range(VECS):
            for j in range(STEPS):
                b = GROUP * j + q
                if a < b < VECS:
                    out[QUAD * q + a][j] = row[min(feature[a], feature[b]), max(feature[a], feature[b])]
    return out


def kernel(**inputs):
    import numpy as np
    import concourse.bacc as bacc
    from concourse.bass_utils import run_bass_kernel_spmd as run

    nc = bacc.Bacc("TRN2", target_bir_lowering=False, num_devices=1)
    arrays = {}

    def give(name, a):
        arrays[name] = np.ascontiguousarray(a)
        return nc.dram_tensor(name, a.shape, mybir.dt.from_np(arrays[name].dtype), kind="ExternalInput").ap()

    w1 = np.asarray(inputs["W_top1"])
    padded = np.concatenate([w1, np.zeros((1, N1), w1.dtype)])
    args = [
        give("x", inputs["r_dense_x"]), give("ids", inputs["ids"]),
        [give(f"tbl_{f}", inputs[f"tbl_{f}"]) for f in range(FIELDS)],
        give("w1_pairs", padded[np.array(pair_rows())]),
        give("w1_dense", w1[-D:]),
        give("b1", np.asarray(inputs["b_top1"]).reshape(C1, P).T),
        give("w2", inputs["W_top2"]),
        give("b2", np.asarray(inputs["b_top2"]).reshape(C2, P).T),
        give("w3", np.asarray(inputs["W_top3"]).reshape(C2, P).T),
    ]
    out = nc.dram_tensor("y", (B, 1), F32, kind="ExternalOutput").ap()
    build(nc, *args, out)
    return run(nc, [arrays], core_ids=[0]).results[0]["y"]
```

```python
from contextlib import ExitStack

import concourse.bass as bass
from concourse import mybir

F32 = mybir.dt.float32
BF16 = mybir.dt.bfloat16
F16 = mybir.dt.float16
I32 = mybir.dt.int32
ALU = mybir.AluOpType
ACT = mybir.ActivationFunctionType

P = 128
B, D = 512, 128
FIELDS = 26
VECS = FIELDS + 1
QUAD = 32
TILES = B // P

PICKED = [0, 5, 8, 12, 15]
SMALL = 1000
ROWS_EACH = 8
SP_ROWS = SMALL // ROWS_EACH
PARTS = 3
GATHERED = [f for f in range(FIELDS) if f not in PICKED]

K = len(PICKED)
ORDER = PICKED + [FIELDS] + GATHERED
AHEAD = K + 1
BLOCKS = [list(range(k, min(k + 4, VECS))) for k in range(AHEAD, VECS, 4)]
NB = len(BLOCKS)
LOW = NB // 2
FIELD_CUT = ORDER[BLOCKS[LOW][0]]
FIRST = ([("lookup", 0), ("block", 0), ("block", 1), ("lookup", 1), ("block", 2), ("lookup", 2), ("block", 3),
          ("lookup", 3), ("block", 4)] + [("block", k) for k in range(5, NB)] + [("lookup", k) for k in range(4, K)])

GROUP = P // QUAD
GROUPS = P // GROUP
STEPS = (VECS + GROUP - 1) // GROUP
COLS = STEPS * GROUP
SPARE = QUAD - VECS
XROWS = GROUP * SPARE * STEPS
FILL = 8
FILLS = GROUPS // FILL
TP = 3
N1, N2 = 512, 256
C1, C2 = N1 // P, N2 // P


def build(nc, x_t, ids, picked_ids, picked_tables, tables, w1, b1, w2, b2, w3, out):
    ids_v = ids.rearrange("(p t) f -> p t f", t=TILES)
    with ExitStack() as ctx:
        def sb(name, shape, dt=F32):
            return ctx.enter_context(nc.sbuf_tensor(name, shape, dt))

        def pb(name, shape):
            return ctx.enter_context(nc.psum_tensor(name, shape, F32))

        def sem(name):
            return ctx.enter_context(nc.semaphore(name))

        row_no = sb("row_no", [P, ROWS_EACH])
        ids_all = sb("ids_all", [P, 2, B], I32)
        ids_f = sb("ids_f", [P, 2, B], F16)
        hot = sb("hot", [P, 2, ROWS_EACH, B], BF16)
        tbl = sb("tbl", [P, 2, ROWS_EACH, D])
        rest = sb("rest", [P, 2, ROWS_EACH, D])
        part = sb("part", [P, 2, PARTS, ROWS_EACH, D], BF16)
        found = sb("found", [D, AHEAD, B])

        ident = sb("ident", [P, P])
        idx = sb("idx", [P, FIELDS], I32)
        rows = sb("rows", [P, VECS - AHEAD, D])
        xt = sb("xt", [D, P, QUAD])
        zt = sb("zt", [P, STEPS, P])
        w1_sb = sb("w1_sb", [P, STEPS, N1])
        w2_sb = sb("w2_sb", [P, C1, N2])
        w3_sb = sb("w3_sb", [P, C2])
        b1_sb = sb("b1_sb", [P, C1])
        b2_sb = sb("b2_sb", [P, C2])
        h1 = sb("h1", [P, C1, P])
        h2 = sb("h2", [P, C2, P])
        y_sb = sb("y_sb", [P, TILES])

        tp = pb("tp", [P, TP, 4, P])
        gram = pb("gram", [P, 2, FILL, P])
        ps2 = pb("ps2", [P, 4, P])

        def lookup_bank(k):
            return gram[:, k % 2, 0:4, :].rearrange("d a b -> d (a b)")

        def chunk(c):
            return gram[:, c // 2, 4 * (c % 2), :]

        s_sp = sem("sp_cleared")
        s_pool = sem("pool_cleared")
        s_act = sem("act_cleared")
        s_zero = sem("ident_zeroed")
        s_ident = sem("ident_ready")
        s_no = sem("row_no_ready")
        s_pad = sem("pads_zeroed")
        s_ids = [sem(f"picked_ids_in_{i}") for i in range(2)]
        s_tbl = [sem(f"picked_table_in_{i}") for i in range(2)]
        s_idf = sem("ids_converted")
        s_hi = sem("part_0_ready")
        s_rest = sem("rest_ready")
        s_mid = sem("part_1_ready")
        s_lo = sem("part_2_ready")
        s_hot = sem("one_hot_ready")
        s_look = sem("looked_up")
        s_found = sem("found_copied")
        s_idx = [sem("idx_low_in"), sem("idx_high_in")]
        s_dense = sem("dense_in")
        s_spare = sem("spare_rows_in")
        s_rows = [sem(f"rows_in_{k}") for k in range(NB)]
        s_w1 = sem("w1_in")
        s_w2 = sem("w2_in")
        s_tr = [sem(f"transposed_{k}") for k in range(NB)]
        s_xt = sem("xt_blocks_ready")
        s_xp = sem("xt_picked_ready")
        s_gram = sem("gram_ready")
        s_za = sem("z_copied_act")
        s_zv = sem("z_copied_dve")
        s_l1 = sem("layer1_ready")
        s_h1 = sem("h1_ready")
        s_l2 = sem("layer2_ready")
        s_h2 = sem("h2_ready")
        s_l3 = sem("layer3_ready")
        s_y = sem("y_ready")
        s_out = sem("out_written")
        block = ctx.enter_context(nc.Block())

        gathers = [16 * len(blk) for blk in BLOCKS]

        def z_copies(copy, f, samples, done):
            b0 = GROUP * FILL * f
            for s in samples:
                for q in range(GROUP):
                    last = copy(
                        zt[QUAD * q:QUAD * q + VECS, :, b0 + s:b0 + GROUP * FILL:GROUP].rearrange("p j g -> p g j"),
                        gram[QUAD * s:QUAD * s + VECS, f % 2, :, s * COLS + q:(s + 1) * COLS:GROUP])
            last.then_inc(done, 1)

        def picked_loads(eng, k):
            eng.dma_start(ids_all[:, k % 2, :],
                          picked_ids[k:k + 1, :].to_broadcast([P, B])).then_inc(s_ids[k % 2], 16)
            eng.dma_start(tbl[0:SP_ROWS, k % 2],
                          picked_tables[k].rearrange("(p c) d -> p c d", c=ROWS_EACH)).then_inc(s_tbl[k % 2], 16)

        def spare_rows(eng, t):
            n = SPARE * STEPS
            for q in range(GROUP):
                eng.dma_start(zt[QUAD * q + VECS:QUAD * (q + 1), :, :],
                              x_t[n * q:n * (q + 1), bass.ds(t, 1), :].rearrange("(i j) t b -> i (j t) b", j=STEPS)
                              ).then_inc(s_spare, 16)

        @block.sync
        def _(sp):
            def low_ids(t):
                sp.dma_start(idx[:, 0:FIELD_CUT], ids_v[:, bass.ds(t, 1), 0:FIELD_CUT]).then_inc(s_idx[0], 16)

            def high_ids(t):
                sp.dma_start(idx[:, FIELD_CUT:], ids_v[:, bass.ds(t, 1), FIELD_CUT:]).then_inc(s_idx[1], 16)

            low_ids(0)
            high_ids(0)
            for k in range(2):
                picked_loads(sp, k)
            sp.dma_start(found[:, K, :], x_t[0:D].rearrange("d t b -> d (t b)")).then_inc(s_dense, 16)
            spare_rows(sp, 0)
            sp.dma_start(w2_sb[:, :, :], w2.rearrange("(c p) n -> p c n", p=P)).then_inc(s_w2, 16)
            sp.dma_start(w3_sb[:, :], w3).then_inc(s_w2, 16)
            sp.dma_start(b1_sb[:, :], b1).then_inc(s_w2, 16)
            sp.dma_start(b2_sb[:, :], b2).then_inc(s_w2, 16)
            with sp.Fori(1, TILES) as t:
                for k in range(LOW):
                    sp.wait_ge(s_rows[k], gathers[k] * t)
                sp.sem_inc(s_sp, 1)
                low_ids(t)
                for k in reversed(range(LOW, NB)):
                    if k < NB - 1:
                        sp.sem_inc(s_sp, 1)
                    sp.wait_ge(s_rows[k], gathers[k] * t)
                sp.sem_inc(s_sp, 1)
                high_ids(t)
            sp.wait_ge(s_y, TILES + 1)
            sp.dma_start(out.rearrange("(p t) o -> p (t o)", t=TILES), y_sb[:, :]).then_inc(s_out, 16)
            sp.wait_ge(s_out, 16)

        @block.gpsimd
        def _(pool):
            pool.iota(row_no[:, :], [[1, ROWS_EACH]], base=0, channel_multiplier=ROWS_EACH,
                      allow_small_or_imprecise_dtypes=True).then_inc(s_no, 1)
            pool.memset(ident[:, :], 0.0).then_inc(s_zero, 1)
            pool.wait_ge(s_zero, 1)
            pool.affine_select(out=ident[:, :], in_=ident[:, :], compare_op=ALU.not_equal, fill=1.0,
                               base=0, pattern=[[-1, P]], channel_multiplier=1).then_inc(s_ident, 1)
            with pool.Fori(0, TILES) as t:
                for k, blk in enumerate(BLOCKS):
                    if k in (0, LOW):
                        pool.wait_ge(s_idx[k // LOW], 16 * t + 16)
                    pool.wait_ge(s_tr[k], t + 1)
                    pool.sem_inc(s_pool, 1)
                    for p in blk:
                        f = ORDER[p]
                        pool.indirect_dma_start(
                            rows[:, p - AHEAD, :], None, tables[f][:, :],
                            bass.IndirectOffsetOnAxis(ap=idx[:, f:f + 1], axis=0),
                        ).then_inc(s_rows[k], 16)

        @block.scalar
        def _(act):
            def copy(dst, src):
                return act.activation(dst, src, ACT.Copy)


            def convert_ids(k):
                i = k % 2
                act.wait_ge(s_ids[i], 16 * (k // 2 + 1))
                if k >= 2:
                    act.wait_ge(s_hot, k - 1)
                copy(ids_f[:, i, :], ids_all[:, i, :]).then_inc(s_idf, 1)

            def part0(k):
                i = k % 2
                act.wait_ge(s_tbl[i], 16 * (k // 2 + 1))
                if k >= 2:
                    act.wait_ge(s_look, k - 1)
                copy(part[0:SP_ROWS, i, 0], tbl[0:SP_ROWS, i]).then_inc(s_hi, 1)

            def part1(k):
                act.wait_ge(s_rest, k + 1)
                copy(part[0:SP_ROWS, k % 2, 1], rest[0:SP_ROWS, k % 2]).then_inc(s_mid, 1)
                if k + 2 < K:
                    act.wait_ge(s_idf, k + 1)
                    picked_loads(act, k + 2)

            act.sem_inc(s_h1, 1)
            act.sem_inc(s_y, 1)
            for k in range(2):
                convert_ids(k)
                part0(k)
            part1(0)
            for k in range(K):
                if k + 1 < K:
                    part1(k + 1)
                if k + 2 < K:
                    convert_ids(k + 2)
                act.wait_ge(s_look, k + 1)
                copy(found[:, k, :], lookup_bank(k)).then_inc(s_found, 1)
                for j in range(k * STEPS // (K - 1), min((k + 1) * STEPS // (K - 1), STEPS)):
                    act.dma_start(w1_sb[:, j, :], w1[:, j, :]).then_inc(s_w1, 16)
                if k + 2 < K:
                    part0(k + 2)
            act.wait_ge(s_found, K)
            act.wait_ge(s_dense, 16)
            act.wait_ge(s_w2, 64)

            def ahead(t):
                copy(xt[:, :, 0:AHEAD].rearrange("d b k -> d k b"),
                     found[:, :, bass.ds(t * P, P)]).then_inc(s_xp, 1)

            def tile(t, last):
                for f in range(FILLS):
                    act.wait_ge(s_gram, FILLS * t + (f + 1))
                    z_copies(copy, f, (0, 1), s_za)
                if not last:
                    ahead(t + 1)
                for c in range(C1):
                    act.wait_ge(s_l1, C1 * t + (c + 1))
                    act.activation(h1[:, c, :], chunk(c), ACT.Relu, bias=b1_sb[:, c:c + 1]).then_inc(s_h1, 1)
                if not last:
                    act.sem_inc(s_act, 1)
                    spare_rows(act, t + 1)
                act.wait_ge(s_l2, t + 1)
                for c in range(C2):
                    act.activation(h2[:, c, :], ps2[:, c, :], ACT.Relu, bias=b2_sb[:, c:c + 1]).then_inc(s_h2, 1)
                act.wait_ge(s_l3, t + 1)
                copy(y_sb[:, bass.ds(t, 1)], ps2[:, C2, 0:1]).then_inc(s_y, 1)

            ahead(0)
            with act.Fori(0, TILES - 1) as t:
                tile(t, False)
            tile(TILES - 1, True)

        @block.vector
        def _(dve):
            dve.memset(xt[:, :, VECS:QUAD], 0.0).then_inc(s_pad, 1)
            dve.wait_ge(s_no, 1)

            def one_hot(k, half):
                if half == 0:
                    dve.wait_ge(s_idf, k + 1)
                    if k >= 2:
                        dve.wait_ge(s_look, k - 1)
                n = ROWS_EACH // 2
                for c in range(n * half, n * (half + 1)):
                    last = dve.tensor_scalar(hot[0:SP_ROWS, k % 2, c, :], ids_f[0:SP_ROWS, k % 2, :],
                                             row_no[0:SP_ROWS, c:c + 1], None, ALU.is_equal)
                if half == 1:
                    last.then_inc(s_hot, 1)

            def left(k, n, before, done):
                whole, to = ((tbl, rest), (rest, part[:, :, PARTS - 1]))[n]
                dve.wait_ge(before, k + 1)
                dve.tensor_tensor(to[0:SP_ROWS, k % 2], whole[0:SP_ROWS, k % 2], part[0:SP_ROWS, k % 2, n],
                                  ALU.subtract).then_inc(done, 1)

            def xt_block(t, k):
                blk = BLOCKS[k]
                dve.wait_ge(s_tr[k], t + 2)
                dve.tensor_copy(xt[:, :, blk[0]:blk[-1] + 1],
                                tp[:, k % TP, 0:len(blk), :].rearrange("d f b -> d b f")).then_inc(s_xt, 1)

            def z_fills(t):
                for f in range(FILLS):
                    dve.wait_ge(s_gram, FILLS * t + (f + 1))
                    z_copies(dve.tensor_copy, f, (2, 3), s_zv)

            def tile(t):
                dve.wait_ge(s_gram, FILLS * t)
                for k in range(NB):
                    xt_block(t, k)
                dve.wait_ge(s_l1, C1 * t)
                z_fills(t)

            one_hot(0, 0)
            one_hot(0, 1)
            left(0, 0, s_hi, s_rest)
            for what, k in FIRST:
                if what == "block":
                    xt_block(0, k)
                    continue
                if k + 1 < K:
                    one_hot(k + 1, 0)
                left(k, 1, s_mid, s_lo)
                if k + 1 < K:
                    one_hot(k + 1, 1)
                    left(k + 1, 0, s_hi, s_rest)
            z_fills(0)
            with dve.Fori(1, TILES) as t:
                tile(t)

        @block.tensor
        def _(pe):
            for k in range(NB):
                pe.sem_inc(s_tr[k], 1)

            def lookup(k):
                i = k % 2
                pe.wait_ge(s_hot, k + 1)
                if k >= 2:
                    pe.wait_ge(s_found, k - 1)
                for n, ready in enumerate((s_hi, s_mid, s_lo)):
                    pe.wait_ge(ready, k + 1)
                    for c in range(ROWS_EACH):
                        last = pe.matmul(lookup_bank(k), part[0:SP_ROWS, i, n, c, :], hot[0:SP_ROWS, i, c, :],
                                         start=n == 0 and c == 0, stop=n == PARTS - 1 and c == ROWS_EACH - 1)
                last.then_inc(s_look, 1)

            def transposes(t, k, follows):
                pe.wait_ge(s_rows[k], gathers[k] * t + gathers[k])
                if k >= TP:
                    pe.wait_ge(s_xt, NB * t + (k - TP + 1))
                elif follows:
                    pe.wait_ge(s_xt, NB * t)
                for i, p in enumerate(BLOCKS[k]):
                    last = pe.transpose(tp[:, k % TP, i, :], rows[:, p - AHEAD, :], ident[:, :])
                last.then_inc(s_tr[k], 1)

            def products(t, f):
                if f >= 2:
                    for done in (s_za, s_zv):
                        pe.wait_ge(done, FILLS * t + (f - 1))
                else:
                    pe.wait_ge(s_h1, C1 * t + 1)
                for g in range(FILL):
                    b0 = (f * FILL + g) * GROUP
                    last = pe.matmul(
                        gram[:, f % 2, g, 0:GROUP * COLS].rearrange("p (s v) -> p s v", s=GROUP),
                        xt[:, b0:b0 + GROUP, :].rearrange("d s v -> d (s v)"),
                        xt[:, b0:b0 + GROUP, 0:COLS], start=True, stop=True)
                last.then_inc(s_gram, 1)

            def layer1(c):
                for j in range(STEPS):
                    last = pe.matmul(chunk(c), w1_sb[:, j, c * P:(c + 1) * P], zt[:, j, :],
                                     start=j == 0, stop=j == STEPS - 1)
                last.then_inc(s_l1, 1)

            def layer2(t, j):
                pe.wait_ge(s_h1, C1 * t + (j + 2))
                for c in range(C2):
                    last = pe.matmul(ps2[:, c, :], w2_sb[:, j, c * P:(c + 1) * P], h1[:, j, :],
                                     start=j == 0 and c == 0, stop=j == C1 - 1, skip_group_check=True)
                if j == C1 - 1:
                    last.then_inc(s_l2, 1)

            def layer3(t):
                pe.wait_ge(s_h2, C2 * t + C2)
                for c in range(C2):
                    last = pe.matmul(ps2[:, C2, 0:1], h2[:, c, :], w3_sb[:, c:c + 1],
                                     start=c == 0, stop=c == C2 - 1)
                last.then_inc(s_l3, 1)

            def open_products(t):
                pe.wait_ge(s_xt, NB * t + NB)
                pe.wait_ge(s_xp, t + 1)
                products(t, 0)

            def layers(t, following):
                steps = iter(following)
                next(steps, None)
                next(steps, None)
                pe.wait_ge(s_spare, 16 * GROUP * t + 16 * GROUP)
                for done in (s_za, s_zv):
                    pe.wait_ge(done, FILLS * t + FILLS)
                layer1(0)
                next(steps, None)
                layer1(1)
                pe.wait_ge(s_y, t + 1)
                for j in range(2, C1):
                    layer2(t, j - 2)
                    layer1(j)
                    next(steps, None)
                layer2(t, C1 - 2)
                next(steps, None)
                layer2(t, C1 - 1)
                for _ in steps:
                    pass

            for what, k in FIRST:
                if what == "lookup":
                    lookup(k)
                else:
                    if k == 0:
                        pe.wait_ge(s_ident, 1)
                    transposes(0, k, False)
            pe.wait_ge(s_pad, 1)
            pe.wait_ge(s_w1, 16 * STEPS)
            pe.wait_ge(s_w2, 64)
            open_products(0)
            with pe.Fori(0, TILES - 1) as t:
                for f in range(1, FILLS):
                    products(t, f)
                layers(t, (transposes(t + 1, k, True) for k in range(NB)))
                open_products(t + 1)
                layer3(t)
            for f in range(1, FILLS):
                products(TILES - 1, f)
            layers(TILES - 1, ())
            layer3(TILES - 1)


def pair_rows():
    row = {}
    for i in range(VECS):
        for j in range(i + 1, VECS):
            row[i, j] = len(row)
    pairs = len(row)
    nothing = pairs + D
    out = [[nothing] * STEPS for _ in range(P)]
    for q in range(GROUP):
        for r in range(QUAD):
            for j in range(STEPS):
                b = GROUP * j + q
                if r >= VECS:
                    out[QUAD * q + r][j] = pairs + min((q * SPARE + r - VECS) * STEPS + j, D)
                elif r < b < VECS:
                    out[QUAD * q + r][j] = row[min(ORDER[r], ORDER[b]), max(ORDER[r], ORDER[b])]
    return out


def kernel(**inputs):
    import numpy as np
    import concourse.bacc as bacc
    from concourse.bass_utils import run_bass_kernel_spmd as run

    nc = bacc.Bacc("TRN2", target_bir_lowering=False, num_devices=1)
    arrays = {}

    def give(name, a):
        arrays[name] = np.ascontiguousarray(a)
        return nc.dram_tensor(name, a.shape, mybir.dt.from_np(arrays[name].dtype), kind="ExternalInput").ap()

    w1 = np.asarray(inputs["W_top1"])
    padded = np.concatenate([w1, np.zeros((1, N1), w1.dtype)])
    ids, x = np.asarray(inputs["ids"]), np.asarray(inputs["r_dense_x"])
    args = [
        give("x_t", np.concatenate([x, np.zeros((B, XROWS - D), x.dtype)], 1).reshape(P, TILES, XROWS).transpose(2, 1, 0)),
        give("ids", ids),
        give("picked_ids", ids.reshape(P, TILES, FIELDS)[:, :, PICKED].transpose(2, 1, 0).reshape(K, B)),
        give("picked_tables", np.stack([np.asarray(inputs[f"tbl_{f}"]) for f in PICKED])),
        {f: give(f"tbl_{f}", inputs[f"tbl_{f}"]) for f in GATHERED},
        give("w1", padded[np.array(pair_rows())]),
        give("b1", np.asarray(inputs["b_top1"]).reshape(C1, P).T),
        give("w2", inputs["W_top2"]),
        give("b2", np.asarray(inputs["b_top2"]).reshape(C2, P).T),
        give("w3", np.asarray(inputs["W_top3"]).reshape(C2, P).T),
    ]
    out = nc.dram_tensor("y", (B, 1), F32, kind="ExternalOutput").ap()
    build(nc, *args, out)
    return run(nc, [arrays], core_ids=[0]).results[0]["y"]
```

```python
from contextlib import ExitStack

import concourse.bass as bass
from concourse import mybir

F32 = mybir.dt.float32
F32R = mybir.dt.float32r
I32 = mybir.dt.int32
ALU = mybir.AluOpType
ACT = mybir.ActivationFunctionType

P = 128
B, D = 512, 128
FIELDS = 26
VECS = FIELDS + 1
QUAD = 32
TILES = B // P

PICKED = [0, 5, 8, 12, 15, 19, 21]
SMALL = 1000
ROWS_EACH = 8
SP_ROWS = SMALL // ROWS_EACH
PARTS = 2
HALF = ROWS_EACH // 2
BY_DVE = ROWS_EACH - 1
GATHERED = [f for f in range(FIELDS) if f not in PICKED]

K = len(PICKED)
ORDER = [FIELDS] + PICKED + GATHERED
AHEAD = K + 1
BLOCKS = [list(range(k, min(k + 4, VECS))) for k in range(AHEAD, VECS, 4)]
NB = len(BLOCKS)
FIRST = ([("lookup", k) for k in range(3)]
         + [("block", 0), ("lookup", 3), ("block", 1), ("block", 2), ("lookup", 4), ("block", 3)]
         + [("lookup", k) for k in range(5, K - 1)] + [("block", k) for k in range(4, NB)] + [("lookup", K - 1)])

GROUP = P // QUAD
GROUPS = P // GROUP
STEPS = VECS // GROUP
BARE = VECS - GROUP * STEPS
FIRSTS = VECS - 1
LOW = BARE - 1
LOW_ROWS = VECS + LOW
HOME = GROUP - 1
GROUP_ROWS = P - QUAD + LOW_ROWS
COLS = VECS - 1
SPARE = QUAD - FIRSTS
SPARES = ([(q, FIRSTS, range(STEPS)) for q in range(HOME)]
          + [(HOME, FIRSTS, range(LOW, STEPS)), (HOME, LOW_ROWS, range(LOW))])
XROWS = sum((QUAD - r) * len(js) for _, r, js in SPARES)
FILL = 8
FILLS = GROUPS // FILL
WARM = 10
TP = 3
N1, N2 = 512, 256
C1, C2 = N1 // P, N2 // P


def build(nc, x_t, ids, picked_ids, picked_tables, tables, w1, b1, w2, b2, w3, out):
    ids_v = ids.rearrange("(p t) f -> p t f", t=TILES)
    with ExitStack() as ctx:
        def sb(name, shape, dt=F32):
            return ctx.enter_context(nc.sbuf_tensor(name, shape, dt))

        def pb(name, shape):
            return ctx.enter_context(nc.psum_tensor(name, shape, F32))

        def sem(name):
            return ctx.enter_context(nc.semaphore(name))

        row_no = sb("row_no", [P, ROWS_EACH])
        last_row = sb("last_row", [P, 1])
        off = sb("off", [P, 2, B])
        ids_all = sb("ids_all", [P, K, B], I32)
        tbl = sb("tbl", [P, K, ROWS_EACH, D])
        hot = sb("hot", [P, 2, ROWS_EACH, B], F32R)
        part = sb("part", [P, 2, PARTS, ROWS_EACH, D], F32R)
        found = sb("found", [D, AHEAD, B])

        ident = sb("ident", [P, P])
        idx = sb("idx", [P, 2, FIELDS], I32)
        rows = sb("rows", [P, VECS - AHEAD, D])
        xt = sb("xt", [D, P, QUAD])
        zt = sb("zt", [P, STEPS, P])
        w1_sb = sb("w1_sb", [P, STEPS, N1])
        w2_sb = sb("w2_sb", [P, C1, N2])
        w3_sb = sb("w3_sb", [P, C2])
        b1_sb = sb("b1_sb", [P, C1])
        b2_sb = sb("b2_sb", [P, C2])
        h1 = sb("h1", [P, C1, P])
        h2 = sb("h2", [P, C2, P])
        y_sb = sb("y_sb", [P, TILES])

        tp = pb("tp", [P, TP, 4, P])
        gram = pb("gram", [P, 2, FILL, P])
        ps2 = pb("ps2", [P, 4, P])

        def lookup_bank(k):
            return gram[:, (k + K) % 2, 0:4, :].rearrange("d a b -> d (a b)")

        def chunk(c):
            return gram[:, c // 2, 4 * (c % 2), :]

        s_pool = sem("pool_cleared")
        s_zero = sem("ident_zeroed")
        s_ident = sem("ident_ready")
        s_no = sem("row_no_ready")
        s_pad = sem("pads_zeroed")
        s_ids = [sem(f"picked_ids_in_{k}") for k in range(K)]
        s_tbl = [sem(f"picked_table_in_{k}") for k in range(K)]
        s_hot = sem("one_hot_ready")
        s_off = sem("distance_ready")
        s_last = sem("last_one_hot_ready")
        s_hi = sem("high_part_ready")
        s_lo = sem("low_part_ready")
        s_look = sem("looked_up")
        s_found = sem("found_copied")
        s_idx = [sem(f"idx_in_{i}") for i in range(2)]
        s_dense = sem("dense_in")
        s_spare = sem("spare_rows_in")
        s_rows = [sem(f"rows_in_{k}") for k in range(NB)]
        s_w1 = sem("w1_in")
        s_w2 = sem("w2_in")
        s_small = sem("w3_and_biases_in")
        s_tr = [sem(f"transposed_{k}") for k in range(NB)]
        s_warm = sem("warmed_up")
        s_xt = sem("xt_blocks_ready")
        s_xp = sem("xt_picked_ready")
        s_gram = sem("gram_ready")
        s_low_a = sem("low_pairs_copied_act")
        s_low_v = sem("low_pairs_copied_dve")
        s_za = sem("z_copied_act")
        s_zv = sem("z_copied_dve")
        s_l1 = sem("layer1_ready")
        s_h1 = sem("h1_ready")
        s_l2 = sem("layer2_ready")
        s_h2 = sem("h2_ready")
        s_l3 = sem("layer3_ready")
        s_y = sem("y_ready")
        s_out = sem("out_written")
        block = ctx.enter_context(nc.Block())

        gathers = [16 * len(blk) for blk in BLOCKS]

        def xt_block(eng, copy, t, k):
            blk = BLOCKS[k]
            eng.wait_ge(s_tr[k], t + 2)
            copy(xt[:, :, blk[0]:blk[-1] + 1], tp[:, k % TP, 0:len(blk), :].rearrange("d f b -> d b f")
                 ).then_inc(s_xt, 1)

        def z_copies(eng, copy, t, f, samples, low_done, done):
            eng.wait_ge(s_gram, FILLS * t + (f + 1))
            b0, b1 = GROUP * FILL * f, GROUP * FILL * (f + 1)
            for s in samples:
                last = copy(
                    zt[QUAD * HOME:QUAD * HOME + LOW_ROWS, 0:LOW, b0 + s:b1:GROUP].rearrange("p j g -> p g j"),
                    gram[QUAD * s:QUAD * s + LOW_ROWS, f % 2, :, s * COLS:s * COLS + LOW])
            last.then_inc(low_done, 1)
            for q in range(GROUP):
                if q == HOME:
                    eng.wait_ge(low_done, FILLS * t + (f + 1))
                for s in samples:
                    last = copy(
                        zt[QUAD * q:QUAD * q + FIRSTS, :, b0 + s:b1:GROUP].rearrange("p j g -> p g j"),
                        gram[QUAD * s:QUAD * s + FIRSTS, f % 2, :,
                             s * COLS + BARE - 1 + q:(s + 1) * COLS:GROUP])
            last.then_inc(done, 1)

        def picked_id_loads(eng, k):
            eng.dma_start(ids_all[:, k, :],
                          picked_ids[k:k + 1, :].to_broadcast([P, B])).then_inc(s_ids[k], 16)

        def picked_table_loads(eng, k):
            eng.dma_start(tbl[0:SP_ROWS, k],
                          picked_tables[k].rearrange("(p c) d -> p c d", c=ROWS_EACH)).then_inc(s_tbl[k], 16)

        def spare_rows(eng, t):
            n = 0
            for q, r, js in SPARES:
                m = (QUAD - r) * len(js)
                eng.dma_start(zt[QUAD * q + r:QUAD * (q + 1), js[0]:js[-1] + 1, :],
                              x_t[n:n + m, t, :].rearrange("(i j) b -> i j b", j=len(js))).then_inc(s_spare, 16)
                n += m

        @block.sync
        def _(sp):
            def row_ids(t):
                sp.dma_start(idx[:, t % 2, :], ids_v[:, t, :]).then_inc(s_idx[t % 2], 16)

            row_ids(0)
            picked_table_loads(sp, 0)
            for k in range(1, K):
                picked_id_loads(sp, k)
                picked_table_loads(sp, k)
            row_ids(1)
            sp.dma_start(found[:, 0, :], x_t[0:D].rearrange("d t b -> d (t b)")).then_inc(s_dense, 16)
            for to, small in ((w3_sb, w3), (b1_sb, b1), (b2_sb, b2)):
                sp.dma_start(to[:, :], small).then_inc(s_small, 16)
            for t in range(1, TILES):
                if t + 1 < TILES:
                    for k in range(NB):
                        sp.wait_ge(s_rows[k], gathers[k] * t)
                    row_ids(t + 1)
                if t == 1:
                    spare_rows(sp, 0)
                    for j in range(STEPS):
                        sp.dma_start(w1_sb[:, j, :], w1[:, j, :]).then_inc(s_w1, 16)
                    sp.dma_start(w2_sb[:, :, :], w2.rearrange("(c p) n -> p c n", p=P)).then_inc(s_w2, 16)
                sp.wait_ge(s_l1, C1 * t)
                spare_rows(sp, t)
            sp.wait_ge(s_y, TILES + 1)
            sp.dma_start(out.rearrange("(p t) o -> p (t o)", t=TILES), y_sb[:, :]).then_inc(s_out, 16)
            sp.wait_ge(s_out, 16)

        @block.gpsimd
        def _(pool):
            pool.iota(row_no[:, :], [[1, ROWS_EACH]], base=0, channel_multiplier=ROWS_EACH,
                      allow_small_or_imprecise_dtypes=True).then_inc(s_no, 1)
            pool.iota(last_row[:, :], [[1, 1]], base=1 - ROWS_EACH, channel_multiplier=-ROWS_EACH,
                      allow_small_or_imprecise_dtypes=True).then_inc(s_no, 1)
            pool.memset(ident[:, :], 0.0).then_inc(s_zero, 1)
            pool.wait_ge(s_zero, 1)
            pool.affine_select(out=ident[:, :], in_=ident[:, :], compare_op=ALU.not_equal, fill=1.0,
                               base=0, pattern=[[-1, P]], channel_multiplier=1).then_inc(s_ident, 1)
            with pool.Fori(0, TILES // 2) as pair:
                for i in range(2):
                    t = 2 * pair + i
                    pool.wait_ge(s_idx[i], 16 * pair + 16)
                    for k, blk in enumerate(BLOCKS):
                        pool.wait_ge(s_tr[k], t + 1)
                        pool.sem_inc(s_pool, 1)
                        for p in blk:
                            f = ORDER[p]
                            pool.indirect_dma_start(
                                rows[:, p - AHEAD, :], None, tables[f][:, :],
                                bass.IndirectOffsetOnAxis(ap=idx[:, i, f:f + 1], axis=0),
                            ).then_inc(s_rows[k], 16)

        @block.scalar
        def _(act):
            def copy(dst, src):
                return act.activation(dst, src, ACT.Copy)

            def high_part(k):
                act.wait_ge(s_tbl[k], 16)
                if k >= 2:
                    act.wait_ge(s_look, k - 1)
                for half in (slice(0, HALF), slice(HALF, ROWS_EACH)):
                    copy(part[0:SP_ROWS, k % 2, 0, half], tbl[0:SP_ROWS, k, half]).then_inc(s_hi, 1)

            def last_one_hot(k):
                act.wait_ge(s_ids[k], 16)
                act.activation(off[0:SP_ROWS, k % 2, :], ids_all[0:SP_ROWS, k, :], ACT.Square,
                               bias=last_row[0:SP_ROWS, :]).then_inc(s_off, 1)
                act.wait_ge(s_off, k + 1)
                if k >= 2:
                    act.wait_ge(s_look, k - 1)
                act.activation(hot[0:SP_ROWS, k % 2, BY_DVE, :], off[0:SP_ROWS, k % 2, :], ACT.Relu,
                               bias=1.0, scale=-1.0).then_inc(s_last, 1)

            picked_id_loads(act, 0)
            act.wait_ge(s_no, 2)
            act.sem_inc(s_h1, 1)
            act.sem_inc(s_y, 1)
            for k in range(2):
                last_one_hot(k)
                high_part(k)
            for what, k in FIRST:
                if what == "block":
                    xt_block(act, copy, 0, k)
                    continue
                act.wait_ge(s_look, k + 1)
                if k == K - 1:
                    copy(xt[:, :, K], lookup_bank(k)[:, 0:P]).then_inc(s_xp, 1)
                copy(found[:, k + 1, :], lookup_bank(k)).then_inc(s_found, 1)
                if k == K - 2:
                    act.wait_ge(s_found, K - 1)
                    act.wait_ge(s_dense, 16)
                    copy(xt[:, :, VECS:LOW_ROWS].rearrange("d b k -> d k b"), found[:, 0:LOW, 0:P])
                    copy(xt[:, :, 0:K].rearrange("d b k -> d k b"), found[:, 0:K, 0:P])
                if k + 2 < K:
                    high_part(k + 2)
                    last_one_hot(k + 2)
            act.wait_ge(s_found, K)
            act.wait_ge(s_small, 48)

            def ahead(t):
                copy(xt[:, :, VECS:LOW_ROWS].rearrange("d b k -> d k b"), found[:, 0:LOW, bass.ds(t * P, P)])
                copy(xt[:, :, 0:AHEAD].rearrange("d b k -> d k b"),
                     found[:, :, bass.ds(t * P, P)]).then_inc(s_xp, 1)

            def z_fills(t):
                for f in range(FILLS):
                    z_copies(act, copy, t, f, (0, 1), s_low_a, s_za)

            def hidden(t):
                for c in range(C1):
                    act.wait_ge(s_l1, C1 * t + (c + 1))
                    act.activation(h1[:, c, :], chunk(c), ACT.Relu, bias=b1_sb[:, c:c + 1]).then_inc(s_h1, 1)
                act.wait_ge(s_l2, t + 1)
                for c in range(C2):
                    act.activation(h2[:, c, :], ps2[:, c, :], ACT.Relu, bias=b2_sb[:, c:c + 1]).then_inc(s_h2, 1)

            def results(t):
                act.wait_ge(s_l3, t + 1)
                copy(y_sb[:, bass.ds(t, 1)], ps2[:, C2, 0:1]).then_inc(s_y, 1)

            z_fills(0)
            with act.Fori(0, TILES - 1) as t:
                ahead(t + 1)
                hidden(t)
                z_fills(t + 1)
                results(t)
            hidden(TILES - 1)
            results(TILES - 1)

        @block.vector
        def _(dve):
            dve.memset(xt[:, :, LOW_ROWS:QUAD], 0.0).then_inc(s_pad, 1)
            dve.wait_ge(s_no, 1)

            def one_hot(k):
                dve.wait_ge(s_ids[k], 16)
                if k >= 2:
                    dve.wait_ge(s_look, k - 1)
                for c in range(BY_DVE):
                    made = dve.tensor_scalar(hot[0:SP_ROWS, k % 2, c, :], ids_all[0:SP_ROWS, k, :],
                                             row_no[0:SP_ROWS, c:c + 1], None, ALU.is_equal)
                    if c in (HALF - 1, BY_DVE - 1):
                        made.then_inc(s_hot, 1)

            def low_part(k):
                dve.wait_ge(s_hi, 2 * k + 2)
                dve.tensor_tensor(part[0:SP_ROWS, k % 2, 1], tbl[0:SP_ROWS, k], part[0:SP_ROWS, k % 2, 0],
                                  ALU.subtract).then_inc(s_lo, 1)

            def z_fills(t):
                for f in range(FILLS):
                    z_copies(dve, dve.tensor_copy, t, f, (2, 3), s_low_v, s_zv)

            def tile(t):
                dve.wait_ge(s_gram, FILLS * t)
                for k in range(NB):
                    xt_block(dve, dve.tensor_copy, t, k)
                dve.wait_ge(s_l1, C1 * t)
                z_fills(t)

            for k in range(K):
                one_hot(k)
                low_part(k)
            z_fills(0)
            with dve.Fori(1, TILES) as t:
                tile(t)

        @block.tensor
        def _(pe):
            for k in range(NB):
                pe.sem_inc(s_tr[k], 1)

            def lookup(k):
                i = k % 2
                if k >= 2:
                    pe.wait_ge(s_found, k - 1)
                for n in range(PARTS):
                    for c in range(ROWS_EACH):
                        if n == 0 and c in (0, HALF):
                            pe.wait_ge(s_hi, 2 * k + 1 + c // HALF)
                            pe.wait_ge(s_hot, 2 * k + 1 + c // HALF)
                        if n == 0 and c == BY_DVE:
                            pe.wait_ge(s_last, k + 1)
                        if n == 1 and c == 0:
                            pe.wait_ge(s_lo, k + 1)
                        last = pe.matmul(lookup_bank(k), part[0:SP_ROWS, i, n, c, :], hot[0:SP_ROWS, i, c, :],
                                         start=n == 0 and c == 0, stop=n == PARTS - 1 and c == ROWS_EACH - 1)
                last.then_inc(s_look, 1)

            def transposes(t, k, follows):
                pe.wait_ge(s_rows[k], gathers[k] * t + gathers[k])
                if k >= TP:
                    pe.wait_ge(s_xt, NB * t + (k - TP + 1))
                elif follows:
                    pe.wait_ge(s_xt, NB * t)
                for i, p in enumerate(BLOCKS[k]):
                    last = pe.transpose(tp[:, k % TP, i, :], rows[:, p - AHEAD, :], ident[:, :])
                last.then_inc(s_tr[k], 1)

            def products(t, f):
                if f >= 2:
                    for done in (s_za, s_zv):
                        pe.wait_ge(done, FILLS * t + (f - 1))
                else:
                    pe.wait_ge(s_h1, C1 * t + 1)
                for g in range(FILL):
                    b0 = (f * FILL + g) * GROUP
                    last = pe.matmul(
                        gram[0:GROUP_ROWS, f % 2, g, 0:GROUP * COLS].rearrange("p (s v) -> p s v", s=GROUP),
                        xt[:, b0:b0 + GROUP, :].rearrange("d s v -> d (s v)")[:, 0:GROUP_ROWS],
                        xt[:, b0:b0 + GROUP, 1:VECS], start=True, stop=True)
                last.then_inc(s_gram, 1)

            def layer1(c):
                for j in range(STEPS):
                    last = pe.matmul(chunk(c), w1_sb[:, j, c * P:(c + 1) * P], zt[:, j, :],
                                     start=j == 0, stop=j == STEPS - 1)
                last.then_inc(s_l1, 1)

            def layer2(t, j):
                pe.wait_ge(s_h1, C1 * t + (j + 2))
                for c in range(C2):
                    last = pe.matmul(ps2[:, c, :], w2_sb[:, j, c * P:(c + 1) * P], h1[:, j, :],
                                     start=j == 0 and c == 0, stop=j == C1 - 1, skip_group_check=True)
                if j == C1 - 1:
                    last.then_inc(s_l2, 1)

            def layer3(t):
                pe.wait_ge(s_h2, C2 * t + C2)
                for c in range(C2):
                    last = pe.matmul(ps2[:, C2, 0:1], h2[:, c, :], w3_sb[:, c:c + 1],
                                     start=c == 0, stop=c == C2 - 1)
                last.then_inc(s_l3, 1)

            def open_products(t):
                pe.wait_ge(s_xt, NB * t + NB)
                pe.wait_ge(s_xp, t + 1)
                products(t, 0)

            def layers(t, following):
                steps = iter(following)
                for _ in range(TP):
                    next(steps, None)
                pe.wait_ge(s_spare, 16 * len(SPARES) * t + 16 * len(SPARES))
                for done in (s_za, s_zv):
                    pe.wait_ge(done, FILLS * t + FILLS)
                layer1(0)
                layer1(1)
                pe.wait_ge(s_y, t + 1)
                for j in range(2, C1):
                    layer2(t, j - 2)
                    layer1(j)
                    next(steps, None)
                layer2(t, C1 - 2)
                layer2(t, C1 - 1)
                for _ in steps:
                    pass

            pe.wait_ge(s_ident, 1)
            for n in range(WARM):
                last = pe.matmul(ps2[:, n % 4, :], ident[:, :], ident[:, :], start=True, stop=True)
            last.then_inc(s_warm, 1)
            for what, k in FIRST:
                if what == "lookup":
                    lookup(k)
                else:
                    transposes(0, k, False)
            pe.wait_ge(s_pad, 1)
            pe.wait_ge(s_warm, 1)
            pe.wait_ge(s_found, K - 1)
            open_products(0)
            pe.wait_ge(s_found, K)
            for f in range(1, FILLS):
                products(0, f)
            pe.wait_ge(s_w1, 16 * STEPS)
            pe.wait_ge(s_w2, 16)
            pe.wait_ge(s_small, 48)
            with pe.Fori(0, TILES - 1) as t:
                layers(t, (transposes(t + 1, k, True) for k in range(NB)))
                open_products(t + 1)
                for f in range(1, FILLS):
                    products(t + 1, f)
                layer3(t)
            layers(TILES - 1, ())
            layer3(TILES - 1)


def pair_rows():
    row = {}
    for i in range(VECS):
        for j in range(i + 1, VECS):
            row[i, j] = len(row)
    pairs = len(row)
    out = [[pairs + D] * STEPS for _ in range(P)]

    def pair(a, b):
        return row[min(ORDER[a], ORDER[b]), max(ORDER[a], ORDER[b])]

    for q in range(GROUP):
        for j in range(STEPS):
            for r in range(min(FIRSTS, BARE + GROUP * j + q)):
                out[QUAD * q + r][j] = pair(r, BARE + GROUP * j + q)
    for j in range(LOW):
        for i in range(j + 1):
            out[QUAD * HOME + VECS + i][j] = pair(i, j + 1)
    n = 0
    for q, r0, js in SPARES:
        for r in range(r0, QUAD):
            for j in js:
                out[QUAD * q + r][j] = pairs + min(n, D)
                n += 1
    return out


def kernel(**inputs):
    import numpy as np
    import concourse.bacc as bacc
    from concourse.bass_utils import run_bass_kernel_spmd as run

    nc = bacc.Bacc("TRN2", target_bir_lowering=False, num_devices=1)
    arrays = {}

    def give(name, a):
        arrays[name] = np.ascontiguousarray(a)
        return nc.dram_tensor(name, a.shape, mybir.dt.from_np(arrays[name].dtype), kind="ExternalInput").ap()

    w1 = np.asarray(inputs["W_top1"])
    padded = np.concatenate([w1, np.zeros((1, N1), w1.dtype)])
    ids, x = np.asarray(inputs["ids"]), np.asarray(inputs["r_dense_x"])
    args = [
        give("x_t", np.concatenate([x, np.zeros((B, XROWS - D), x.dtype)], 1).reshape(P, TILES, XROWS).transpose(2, 1, 0)),
        give("ids", ids),
        give("picked_ids", ids.reshape(P, TILES, FIELDS)[:, :, PICKED].transpose(2, 1, 0).reshape(K, B)),
        give("picked_tables", np.stack([np.asarray(inputs[f"tbl_{f}"]) for f in PICKED])),
        {f: give(f"tbl_{f}", inputs[f"tbl_{f}"]) for f in GATHERED},
        give("w1", padded[np.array(pair_rows())]),
        give("b1", np.asarray(inputs["b_top1"]).reshape(C1, P).T),
        give("w2", inputs["W_top2"]),
        give("b2", np.asarray(inputs["b_top2"]).reshape(C2, P).T),
        give("w3", np.asarray(inputs["W_top3"]).reshape(C2, P).T),
    ]
    out = nc.dram_tensor("y", (B, 1), F32, kind="ExternalOutput").ap()
    build(nc, *args, out)
    return run(nc, [arrays], core_ids=[0]).results[0]["y"]
```
